# Optimizing a Trainium2 kernel written in Bass

```python
import numpy as np
import jax
import jax.numpy as jnp

def _softmax(x, axis=-1):
    return jax.nn.softmax(x, axis=axis)

def _gelu(x):
    return jax.nn.gelu(x, approximate=True)

def _silu(x):
    return jax.nn.silu(x)

def _sigmoid(x):
    return jax.nn.sigmoid(x)

def _layernorm(x, axis=-1, eps=1e-05):
    m = jnp.mean(x, axis=axis, keepdims=True)
    v = jnp.var(x, axis=axis, keepdims=True)
    return (x - m) / jnp.sqrt(v + eps)

def _scatter_add(tgt, idx, src, axis=0):
    return tgt.at[idx].add(src)

def _segment_sum(src, seg, n):
    return jax.ops.segment_sum(src, seg, n)
kernel_name = 'mk_macaron_d1_jaxref_r8_e05bc9'

def setup_inputs(seed: int=0):
    np.random.seed(seed)
    _w = jnp.asarray

    def _L0_attn_setup():
        import jax, jax.numpy as jnp
        import numpy as np
        B, N, DIM = (4, 128, 128)
        H, DH = (16, 64)
        NUM_MEM = 4
        TOPK = 64
        QK_SCALE = 10.0

        def l2norm(t, eps=1e-12):
            return t / jnp.clip(jnp.linalg.norm(t, axis=-1, keepdims=True), eps)
        key = jax.random.key(seed)
        ks = jax.random.split(key, 12)
        s = 0.02
        inp = {'x': jax.random.normal(ks[0], (B, N, DIM), dtype=jnp.float32), 'Wq': jax.random.normal(ks[1], (DIM, H * DH), dtype=jnp.float32) * s, 'Wk': jax.random.normal(ks[2], (DIM, H * DH), dtype=jnp.float32) * s, 'Wv': jax.random.normal(ks[3], (DIM, H * DH), dtype=jnp.float32) * s, 'W_pre_th': jax.random.normal(ks[4], (H, H), dtype=jnp.float32) * (1.0 / H) ** 0.5, 'W_post_th': jax.random.normal(ks[5], (H, H), dtype=jnp.float32) * (1.0 / H) ** 0.5, 'mem_k': jax.random.normal(ks[6], (H, NUM_MEM, DH), dtype=jnp.float32), 'mem_v': jax.random.normal(ks[7], (H, NUM_MEM, DH), dtype=jnp.float32), 'head_scale_params': jnp.ones((1, H, 1, 1), dtype=jnp.float32), 'Wg': jax.random.normal(ks[8], (DIM, H * DH), dtype=jnp.float32) * s, 'bg': jnp.ones((H * DH,), dtype=jnp.float32), 'Wo': jax.random.normal(ks[9], (H * DH, DIM), dtype=jnp.float32) * s}
        return inp
    _L0_attn_in = _L0_attn_setup()

    def _L0_ffn_setup():
        import jax, jax.numpy as jnp
        import numpy as np
        BLOCK = 16
        _GRID = jnp.array([0.0, 0.5, 1.0, 1.5, 2.0, 3.0, 4.0, 6.0], dtype=jnp.float32)
        _MID = jnp.array([0.25, 0.75, 1.25, 1.75, 2.5, 3.5, 5.0], dtype=jnp.float32)

        def fp4_quant_dequant(x):
            shape = x.shape
            xb = x.reshape(shape[:-1] + (shape[-1] // BLOCK, BLOCK))
            scale = jnp.max(jnp.abs(xb), axis=-1, keepdims=True) / 6.0
            scale = jnp.maximum(scale, jnp.float32(1e-12))
            xn = xb / scale
            idx = jnp.searchsorted(_MID, jnp.abs(xn))
            q = _GRID[idx] * jnp.sign(xn) * scale
            return q.reshape(shape)

        def fp4_linear(x, w):
            xq = fp4_quant_dequant(x)
            wq = fp4_quant_dequant(w)
            return jnp.einsum('bsk,nk->bsn', xq, wq)
        key = jax.random.key(seed)
        k1, k2, k3, k4 = jax.random.split(key, 4)
        H, I = (128, 352)
        x = jax.random.normal(k1, (4, 512, H), dtype=jnp.float32)
        w_gate = jax.random.normal(k2, (I, H), dtype=jnp.float32) * 0.02
        w_up = jax.random.normal(k3, (I, H), dtype=jnp.float32) * 0.02
        w_down = jax.random.normal(k4, (H, I), dtype=jnp.float32) * 0.02
        return {'x': x, 'w_gate': w_gate, 'w_up': w_up, 'w_down': w_down}
    _L0_ffn_in = _L0_ffn_setup()
    _d = {'L0_attn_x': _L0_attn_in['x'], 'L0_attn_Wq': _L0_attn_in['Wq'], 'L0_attn_Wk': _L0_attn_in['Wk'], 'L0_attn_Wv': _L0_attn_in['Wv'], 'L0_attn_W_pre_th': _L0_attn_in['W_pre_th'], 'L0_attn_W_post_th': _L0_attn_in['W_post_th'], 'L0_attn_mem_k': _L0_attn_in['mem_k'], 'L0_attn_mem_v': _L0_attn_in['mem_v'], 'L0_attn_head_scale_params': _L0_attn_in['head_scale_params'], 'L0_attn_Wg': _L0_attn_in['Wg'], 'L0_attn_bg': _L0_attn_in['bg'], 'L0_attn_Wo': _L0_attn_in['Wo'], 'L0_ffn_w_gate': _L0_ffn_in['w_gate'], 'L0_ffn_w_up': _L0_ffn_in['w_up'], 'L0_ffn_w_down': _L0_ffn_in['w_down']}
    _x0 = _d['L0_attn_x']
    _d['L0_attn_x'] = jax.random.normal(jax.random.fold_in(jax.random.key(seed), 1), (2, 1024, 128), dtype=_x0.dtype)
    del _x0
    return _d

def reference(L0_attn_x, L0_attn_Wq, L0_attn_Wk, L0_attn_Wv, L0_attn_W_pre_th, L0_attn_W_post_th, L0_attn_mem_k, L0_attn_mem_v, L0_attn_head_scale_params, L0_attn_Wg, L0_attn_bg, L0_attn_Wo, L0_ffn_w_gate, L0_ffn_w_up, L0_ffn_w_down):

    def _L0_attn_ref(x, Wq, Wk, Wv, W_pre_th, W_post_th, mem_k, mem_v, head_scale_params, Wg, bg, Wo):
        import jax, jax.numpy as jnp
        import numpy as np
        B, N, DIM = (4, 128, 128)
        H, DH = (16, 64)
        NUM_MEM = 4
        TOPK = 64
        QK_SCALE = 10.0

        def l2norm(t, eps=1e-12):
            return t / jnp.clip(jnp.linalg.norm(t, axis=-1, keepdims=True), eps)
        b, n, _ = x.shape
        q = (x @ Wq).reshape(b, n, H, DH).transpose(0, 2, 1, 3)
        k = (x @ Wk).reshape(b, n, H, DH).transpose(0, 2, 1, 3)
        v = (x @ Wv).reshape(b, n, H, DH).transpose(0, 2, 1, 3)
        mk = jnp.broadcast_to(mem_k[None], (b, H, NUM_MEM, DH))
        mv = jnp.broadcast_to(mem_v[None], (b, H, NUM_MEM, DH))
        k = jnp.concatenate([mk, k], axis=2)
        v = jnp.concatenate([mv, v], axis=2)
        q = l2norm(q)
        k = l2norm(k)
        dots = jnp.einsum('bhid,bhjd->bhij', q, k) * QK_SCALE
        dots = jnp.einsum('hg,bgij->bhij', W_pre_th, dots)
        mask_value = -jnp.finfo(dots.dtype).max
        j = n + NUM_MEM
        col_pos = jnp.arange(j) - NUM_MEM
        causal = jnp.arange(n)[:, None] < col_pos[None, :]
        dots = jnp.where(causal[None, None], mask_value, dots)
        top = jax.lax.top_k(dots, TOPK)[0]
        vk = top[..., -1:]
        dots = jnp.where(dots < vk, mask_value, dots)
        attn = jax.nn.softmax(dots, axis=-1)
        attn = jnp.einsum('hg,bgij->bhij', W_post_th, attn)
        out = jnp.einsum('bhij,bhjd->bhid', attn, v)
        out = out * head_scale_params
        out = out.transpose(0, 2, 1, 3).reshape(b, n, H * DH)
        gates = x @ Wg + bg
        out = out * jax.nn.sigmoid(gates)
        return out @ Wo

    def _L0_ffn_ref(x, w_gate, w_up, w_down):
        import jax, jax.numpy as jnp
        import numpy as np
        BLOCK = 16
        _GRID = jnp.array([0.0, 0.5, 1.0, 1.5, 2.0, 3.0, 4.0, 6.0], dtype=jnp.float32)
        _MID = jnp.array([0.25, 0.75, 1.25, 1.75, 2.5, 3.5, 5.0], dtype=jnp.float32)

        def fp4_quant_dequant(x):
            shape = x.shape
            xb = x.reshape(shape[:-1] + (shape[-1] // BLOCK, BLOCK))
            scale = jnp.max(jnp.abs(xb), axis=-1, keepdims=True) / 6.0
            scale = jnp.maximum(scale, jnp.float32(1e-12))
            xn = xb / scale
            idx = jnp.searchsorted(_MID, jnp.abs(xn))
            q = _GRID[idx] * jnp.sign(xn) * scale
            return q.reshape(shape)

        def fp4_linear(x, w):
            xq = fp4_quant_dequant(x)
            wq = fp4_quant_dequant(w)
            return jnp.einsum('bsk,nk->bsn', xq, wq)
        gate = fp4_linear(x, w_gate)
        y = fp4_linear(x, w_up)
        h = jax.nn.silu(gate) * y
        return fp4_linear(h, w_down)
    x = L0_attn_x
    x = x + 0.5 * _L0_ffn_ref(_layernorm(x, axis=-1), L0_ffn_w_gate, L0_ffn_w_up, L0_ffn_w_down)
    x = x + _L0_attn_ref(_layernorm(x, axis=-1), L0_attn_Wq, L0_attn_Wk, L0_attn_Wv, L0_attn_W_pre_th, L0_attn_W_post_th, L0_attn_mem_k, L0_attn_mem_v, L0_attn_head_scale_params, L0_attn_Wg, L0_attn_bg, L0_attn_Wo)
    x = x + 0.5 * _L0_ffn_ref(_layernorm(x, axis=-1), L0_ffn_w_gate, L0_ffn_w_up, L0_ffn_w_down)
    return x

_drawn_inputs = setup_inputs


def setup_inputs(seed=0):
    import zlib

    import numpy as np

    out = dict(_drawn_inputs(seed))
    spreads = {'L0_attn_head_scale_params': (1.0, 0.6), 'L0_attn_bg': (1.0, 0.6)}
    factors = {'L0_attn_mem_k': 2.853,
     'L0_attn_Wg': 8.0,
     'L0_ffn_w_gate': 5.525,
     'L0_ffn_w_up': 5.26,
     'L0_ffn_w_down': 5.276}
    for name, (base, spread) in spreads.items():
        noise = np.random.default_rng([zlib.crc32(name.encode()), seed]).standard_normal(out[name].shape)
        drawn = base * np.exp(spread * noise) if base else spread * noise
        out[name] = jnp.asarray(drawn.astype(out[name].dtype))
    for name, factor in factors.items():
        out[name] = (out[name] * factor).astype(out[name].dtype)
    return out
```

```python
from contextlib import ExitStack

import concourse.bass as bass
from concourse import mybir

ALU = mybir.AluOpType
ACT = mybir.ActivationFunctionType
F32 = mybir.dt.float32
BF16 = mybir.dt.bfloat16
U32 = mybir.dt.uint32
AX_X = mybir.AxisListType.X

P = 128
BANK = 512
NEG = -3.0e38
GONE = -3.39e38
LN_EPS = 1e-5
NORM_EPS = 1e-12
TOPK = 64
QK_SCALE = 10.0
QBLOCK = 16


def pieces(width):
    n = -(-width // BANK)
    step = -(-width // (4 * n)) * 4
    return [(a, min(step, width - a)) for a in range(0, width, step)]


def chunks(width):
    return [(a, min(P, width - a)) for a in range(0, width, P)]


class Counter:

    def __init__(self, engine, sem):
        self.engine, self.sem, self.n = engine, sem, 0

    def link(self, instruction):
        self.n += 1
        instruction.then_inc(self.sem, 1)
        self.engine.wait_ge(self.sem, self.n)


def quantise_scale(link, v, src, amax, scale, rscale):
    link(v.tensor_reduce(amax, src, AX_X, ALU.max, apply_absolute_value=True))
    link(v.tensor_scalar(scale, amax, 1.0 / 6.0, 1e-12, ALU.mult, ALU.max))
    link(v.reciprocal(rscale, scale))


def quantise_levels(link, v, a, level, tmp):
    link(v.tensor_scalar(level, a, 5.0, 2.0, ALU.is_gt, ALU.mult))
    link(v.scalar_tensor_tensor(out=level, in0=a, scalar=3.5, in1=level, op0=ALU.is_gt, op1=ALU.add))
    link(v.scalar_tensor_tensor(out=level, in0=a, scalar=2.5, in1=level, op0=ALU.is_gt, op1=ALU.add))
    link(v.tensor_scalar(tmp, a, 1.75, None, ALU.is_gt))
    for mid in (1.25, 0.75, 0.25):
        link(v.scalar_tensor_tensor(out=tmp, in0=a, scalar=mid, in1=tmp, op0=ALU.is_gt, op1=ALU.add))
    link(v.scalar_tensor_tensor(out=level, in0=tmp, scalar=0.5, in1=level, op0=ALU.mult, op1=ALU.add))


def macaron_kernel(nc, x, wq, wk, wv, wpreT, wpostT, mem_k, mem_v, head_scale, wg, bg, wo,
                   w_gate, w_up, w_down, out):
    B, N, D = x.shape
    H = wpreT.shape[0]
    HD = wq.shape[1]
    DH = HD // H
    MEM = mem_k.shape[0]
    I = w_gate.shape[0]
    NT = N // P
    PAIRS = H // 2
    J = N + MEM
    UNITS = N // 64
    G = 8
    KC = len(chunks(J))
    BLK_X = D // QBLOCK
    BLK_H = I // QBLOCK
    HB = 4
    ICH = chunks(I)
    assert D == P and 2 * DH == P and H * G == P

    all_sems = []

    with ExitStack() as ctx:
        def sb(stack, name, shape, dt=F32):
            return stack.enter_context(nc.sbuf_tensor(name, shape, dt))

        def ps(stack, name, shape, dt=F32):
            return stack.enter_context(nc.psum_tensor(name, shape, dt))

        def sem(name):
            s = nc.alloc_semaphore(name)
            all_sems.append(s)
            return s

        q_dram = nc.dram_tensor("q_scratch", (UNITS, P, PAIRS, 64), F32, kind="Internal").ap()
        gate_dram = nc.dram_tensor("gate_scratch", (P, PAIRS, N), F32, kind="Internal").ap()
        w_gu_dram = nc.dram_tensor("w_gu_scratch", (P, 2 * I), F32, kind="Internal").ap()
        w_dn_dram = nc.dram_tensor("w_dn_scratch", (P, len(ICH), P), F32, kind="Internal").ap()

        ident = sb(ctx, "ident", [P, P])
        mix_pre = sb(ctx, "mix_pre", [P, P])
        mix_post = sb(ctx, "mix_post", [P, P])
        row_sel = sb(ctx, "row_sel", [G, P], BF16)
        row_mask = sb(ctx, "row_mask", [G, G, 64], BF16)
        x_sb = sb(ctx, "x_sb", [P, NT, D])

        setup_weights(nc, ctx, sb, ps, sem, ident, mix_pre, mix_post, row_sel, row_mask, wpreT, wpostT,
                      w_gate, w_up, w_down, w_gu_dram, w_dn_dram, I, ICH, BLK_X, BLK_H, G, H)
        first_loop_sem = len(all_sems)

        def layer_norm(v, link, rows, stats, mv, std, rstd, xn, var_ready, std_ready):
            for t in rows:
                ins = v.bn_stats(stats[:, t, :], x_sb[:, t, :])
            link(ins)
            for t in rows:
                ins = v.bn_aggr(mv[:, t, :], stats[:, t, :])
            link(ins)
            v.tensor_scalar(std[:, :], mv[:, :, 1], LN_EPS, None, ALU.add).then_inc(var_ready, 1)
            nc.vector.wait_ge(std_ready, 1)
            link(v.reciprocal(rstd[:, :], std[:, :]))
            for t in rows:
                ins = v.tensor_scalar(xn[:, t, :], x_sb[:, t, :], mv[:, t, 0:1], rstd[:, t:t + 1],
                                      ALU.subtract, ALU.mult)
            return ins

        def ffn(b, phase):
            first, final = phase == 0, phase == 1
            nm = f"f{phase}_"
            with ExitStack() as f:
                w_gu = sb(f, nm + "w_gu", [P, 2 * I])
                w_dn = sb(f, nm + "w_dn", [P, len(ICH), P])
                stats = sb(f, nm + "stats", [P, NT, 6])
                mv = sb(f, nm + "mv", [P, NT, 2])
                std = sb(f, nm + "std", [P, NT])
                rstd = sb(f, nm + "rstd", [P, NT])
                xn = sb(f, nm + "xn", [P, NT * D])
                xs = sb(f, nm + "xs", [P, HB * I])
                mag = sb(f, nm + "mag", [P, HB * I])
                sign = sb(f, nm + "sign", [P, HB * I])
                level = sb(f, nm + "level", [P, HB * I])
                tmp = sb(f, nm + "tmp", [P, HB * I])
                xq = sb(f, nm + "xq", [P, NT * D])
                hq = sb(f, nm + "hq", [P, HB * I])
                amax = sb(f, nm + "amax", [P, HB * BLK_H])
                scale = sb(f, nm + "scale", [P, HB * BLK_H])
                rscale = sb(f, nm + "rscale", [P, HB * BLK_H])
                xqT = sb(f, nm + "xqT", [P, NT, P])
                sig = sb(f, nm + "sig", [P, 2, I])
                hid = sb(f, nm + "hid", [P, HB * I])
                hqT = sb(f, nm + "hqT", [P, 2, len(ICH), P])
                tp = ps(f, nm + "tp", [P, 2, BANK])
                gp = ps(f, nm + "gp", [P, 2, BANK])
                up = ps(f, nm + "up", [P, 2, BANK])
                dp = ps(f, nm + "dp", [P, BANK])

                loaded = sem(nm + "loaded")
                weights_in = sem(nm + "weights_in")
                dve_step = sem(nm + "dve_step")
                var_ready = sem(nm + "var_ready")
                std_ready = sem(nm + "std_ready")
                scaled = sem(nm + "scaled")
                mag_ready = sem(nm + "mag_ready")
                sign_ready = sem(nm + "sign_ready")
                sign_scaled = sem(nm + "sign_scaled")
                xq_ready = sem(nm + "xq_ready")
                xT_ready = sem(nm + "xT_ready")
                xqT_ready = sem(nm + "xqT_ready")
                gu_ready = sem(nm + "gu_ready")
                sig_ready = sem(nm + "sig_ready")
                hid_done = sem(nm + "hid_done")
                down_made = sem(nm + "down_made")
                hq_ready = sem(nm + "hq_ready")
                hT_ready = sem(nm + "hT_ready")
                hqT_ready = sem(nm + "hqT_ready")
                down_ready = sem(nm + "down_ready")
                x_updated = sem(nm + "x_updated")
                stored = sem(nm + "stored")

                NX = NT * D
                NH = HB * I
                sizes = [NX] + [NH] * (NT // HB)

                block = f.enter_context(nc.Block())

                @block.sync
                def _(sp):
                    if first:
                        sp.dma_start(x_sb[:, :, :], x[b].rearrange("(t p) d -> p t d", p=P)).then_inc(loaded, 16)
                    sp.dma_start(w_gu[:, :], w_gu_dram).then_inc(weights_in, 16)
                    sp.dma_start(w_dn[:, :, :], w_dn_dram).then_inc(weights_in, 16)
                    if final:
                        sp.wait_ge(x_updated, NT // HB)
                        sp.dma_start(out[b].rearrange("(t p) d -> p t d", p=P), x_sb[:, :, :]).then_inc(stored, 16)
                        sp.wait_ge(stored, 16)

                @block.vector
                def _(dve):
                    v = nc.vector
                    steps = Counter(dve, dve_step)
                    if first:
                        dve.wait_ge(loaded, 16)
                    steps.link(layer_norm(v, steps.link, range(NT), stats, mv, std, rstd,
                                          xn[:, :].rearrange("p (t d) -> p t d", d=D), var_ready, std_ready))

                    def quantise(k, src, dst, n):
                        blocks = n // QBLOCK
                        s3 = src[:, 0:n].rearrange("p (n e) -> p n e", e=QBLOCK)
                        if k >= 1:
                            dve.wait_ge(sign_scaled, k)
                        quantise_scale(steps.link, v, s3, amax[:, 0:blocks], scale[:, 0:blocks], rscale[:, 0:blocks])
                        if k >= 1:
                            dve.wait_ge(sign_ready, k)
                        v.tensor_tensor(xs[:, 0:n].rearrange("p (n e) -> p n e", e=QBLOCK), s3,
                                        rscale[:, 0:blocks].unsqueeze(2).to_broadcast([P, blocks, QBLOCK]),
                                        ALU.mult).then_inc(scaled, 1)
                        dve.wait_ge(mag_ready, k + 1)
                        quantise_levels(steps.link, v, mag[:, 0:n], level[:, 0:n], tmp[:, 0:n])
                        dve.wait_ge(sign_scaled, k + 1)
                        return v.tensor_tensor(dst[:, 0:n], level[:, 0:n], sign[:, 0:n], ALU.mult)

                    quantise(0, xn, xq, NX).then_inc(xq_ready, 1)
                    for k in range(NT // HB):
                        for t in range(HB * k, HB * (k + 1)):
                            dve.wait_ge(gu_ready, t + 1)
                            dve.wait_ge(sig_ready, t + 1)
                            s = sig[:, t % 2, :]
                            steps.link(v.tensor_tensor(s, gp[:, t % 2, 0:I], s, ALU.mult))
                            ins = v.tensor_tensor(hid[:, (t % HB) * I:(t % HB + 1) * I], s, up[:, t % 2, 0:I], ALU.mult)
                            ins.then_inc(hid_done, 1)
                        dve.wait_ge(hid_done, HB * (k + 1))
                        if k >= 1:
                            dve.wait_ge(hT_ready, HB * k)
                        quantise(1 + k, hid, hq, NH).then_inc(hq_ready, 1)
                        dve.wait_ge(down_ready, k + 1)
                        rows = x_sb[:, HB * k:HB * (k + 1), :]
                        v.scalar_tensor_tensor(out=rows, in0=dp[:, :].rearrange("p (t d) -> p t d", d=D), scalar=0.5,
                                               in1=rows, op0=ALU.mult, op1=ALU.add).then_inc(x_updated, 1)

                @block.gpsimd
                def _(pool):
                    for k, n in enumerate(sizes):
                        pool.wait_ge(sign_ready, k + 1)
                        s3 = sign[:, 0:n].rearrange("p (n e) -> p n e", e=QBLOCK)
                        nc.gpsimd.tensor_tensor(s3, s3, scale[:, 0:n // QBLOCK].unsqueeze(2).to_broadcast(
                            [P, n // QBLOCK, QBLOCK]), ALU.mult).then_inc(sign_scaled, 1)

                @block.scalar
                def _(act):
                    a = nc.scalar

                    def magnitudes(k):
                        n = sizes[k]
                        act.wait_ge(scaled, k + 1)
                        a.activation(mag[:, 0:n], xs[:, 0:n], ACT.Abs).then_inc(mag_ready, 1)
                        if k >= 1:
                            act.wait_ge([xq_ready, hq_ready][k > 1], max(1, k - 1))
                        a.activation(sign[:, 0:n], xs[:, 0:n], ACT.Sign).then_inc(sign_ready, 1)

                    act.wait_ge(var_ready, 1)
                    a.activation(std[:, :], std[:, :], ACT.Sqrt).then_inc(std_ready, 1)
                    magnitudes(0)
                    for k in range(2):
                        act.wait_ge(xT_ready, k + 1)
                        a.activation(xqT[:, 4 * k:4 * k + 4, :], tp[:, k, :].rearrange("p (t d) -> p t d", d=P),
                                     ACT.Copy).then_inc(xqT_ready, 1)
                    for k in range(NT // HB):
                        for t in range(HB * k, HB * (k + 1)):
                            act.wait_ge(gu_ready, t + 1)
                            if t >= 2:
                                act.wait_ge(hid_done, t - 1)
                            a.activation(sig[:, t % 2, :], gp[:, t % 2, 0:I], ACT.Sigmoid).then_inc(sig_ready, 1)
                        magnitudes(1 + k)
                        for t in range(HB * k, HB * (k + 1)):
                            act.wait_ge(hT_ready, t + 1)
                            if t >= 2:
                                act.wait_ge(down_made, t - 1)
                            full = len(ICH) - 1
                            a.activation(hqT[:, t % 2, 0:full, :], tp[:, t % 2, 0:full * P].rearrange(
                                "p (c d) -> p c d", d=P), ACT.Copy)
                            r = ICH[-1][1]
                            a.activation(hqT[0:r, t % 2, full, :], tp[0:r, t % 2, full * P:(full + 1) * P],
                                         ACT.Copy).then_inc(hqT_ready, 1)

                @block.tensor
                def _(pe):
                    te = nc.tensor
                    pe.wait_ge(xq_ready, 1)
                    for t in range(NT):
                        ins = te.transpose(tp[:, t // 4, (t % 4) * P:(t % 4 + 1) * P], xq[:, t * D:(t + 1) * D],
                                           ident[:, :])
                        if t % 4 == 3:
                            ins.then_inc(xT_ready, 1)
                    pe.wait_ge(weights_in, 32)

                    def gate_up(t):
                        pe.wait_ge(xqT_ready, t // 4 + 1)
                        if t >= 2:
                            pe.wait_ge(hid_done, t - 1)
                        te.matmul(gp[:, t % 2, 0:I], xqT[:, t, :], w_gu[:, 0:I], start=True, stop=True)
                        te.matmul(up[:, t % 2, 0:I], xqT[:, t, :], w_gu[:, I:2 * I], start=True,
                                  stop=True).then_inc(gu_ready, 1)

                    for k in range(NT // HB):
                        for t in range(HB * k, HB * (k + 1)):
                            gate_up(t)
                        pe.wait_ge(hq_ready, k + 1)

                        def turn(t):
                            if t >= 2:
                                pe.wait_ge(hqT_ready, t - 1)
                            else:
                                pe.wait_ge(xqT_ready, 2)
                            for c, (a0, m) in enumerate(ICH):
                                o = (t % HB) * I + a0
                                ins = te.transpose(tp[0:m, t % 2, c * P:(c + 1) * P], hq[:, o:o + m], ident[:, :])
                            ins.then_inc(hT_ready, 1)

                        turn(HB * k)
                        for t in range(HB * k, HB * (k + 1)):
                            if t + 1 < HB * (k + 1):
                                turn(t + 1)
                            pe.wait_ge(hqT_ready, t + 1)
                            if k >= 1:
                                pe.wait_ge(x_updated, k)
                            for c, (a0, m) in enumerate(ICH):
                                ins = te.matmul(dp[:, (t % HB) * P:(t % HB + 1) * P], hqT[0:m, t % 2, c, :],
                                                w_dn[0:m, c, :], start=(c == 0), stop=(c == len(ICH) - 1))
                            ins.then_inc(down_made, 1)
                        pe.wait_ge(down_made, HB * (k + 1))
                        pe.sem_inc(down_ready, 1)

        def project(b, kT, v_sb):
            with ExitStack() as f:
                w = [sb(f, f"p_w{n}", [P, HD]) for n in "vkqg"]
                memv = sb(f, "p_memv", [MEM, HD])
                memk = sb(f, "p_memk", [MEM, HD])
                bias = sb(f, "p_bias", [P, PAIRS])
                hscale = sb(f, "p_hscale", [P, PAIRS])
                stats = sb(f, "p_stats", [P, NT, 6])
                mv = sb(f, "p_mv", [P, NT, 2])
                std = sb(f, "p_std", [P, NT])
                rstd = sb(f, "p_rstd", [P, NT])
                xn = sb(f, "p_xn", [P, NT, D])
                xT = sb(f, "p_xT", [P, J])
                sq = sb(f, "p_sq", [P, 2, HD])
                ss = sb(f, "p_ss", [P, 2, H])
                nrm = sb(f, "p_nrm", [P, 2, H])
                rnrm = sb(f, "p_rnrm", [P, 2, H])
                rows_n = sb(f, "p_rows_n", [P, 2, HD])
                q_out = sb(f, "p_q_out", [P, 2, PAIRS, P])
                gates = sb(f, "p_gates", [P, 2, N])
                proj = ps(f, "p_proj", [P, 2, 2 * BANK])
                turned = ps(f, "p_turned", [P, 2, 2 * BANK])

                inputs_in = sem("p_weights_in")
                dve_step = sem("p_dve_step")
                var_ready = sem("p_var_ready")
                std_ready = sem("p_std_ready")
                zero_ready = sem("p_zero_ready")
                xn_ready = sem("p_xn_ready")
                xnT_ready = sem("p_xnT_ready")
                xT_ready = sem("p_xT_ready")
                proj_ready = sem("p_proj_ready")
                proj_read = sem("p_proj_read")
                sq_ready = sem("p_sq_ready")
                ss_ready = sem("p_ss_ready")
                nrm_ready = sem("p_nrm_ready")
                rows_ready = sem("p_rows_ready")
                turned_ready = sem("p_turned_ready")
                turned_read = sem("p_turned_read")
                q_stored = [sem(f"p_q_stored{k}") for k in range(2)]
                g_sig = sem("p_g_sig")
                g_ready = sem("p_g_ready")
                g_stored = [sem(f"p_g_stored{k}") for k in range(2)]

                tiles = ([("v", c, m) for c, (_, m) in enumerate(chunks(J))]
                         + [("k", c, m) for c, (_, m) in enumerate(chunks(J))]
                         + [("q", c, P) for c in range(NT)] + [("g", p, P) for p in range(PAIRS)])
                normed = [n for n, (kind, _, _) in enumerate(tiles) if kind in "kq"]
                order = {n: k for k, n in enumerate(normed)}

                block = f.enter_context(nc.Block())

                @block.sync
                def _(sp):
                    for dst, src in zip(w, (wv, wk, wq, wg)):
                        sp.dma_start(dst[:, :], src).then_inc(inputs_in, 16)
                    sp.dma_start(memk[:, :], mem_k).then_inc(inputs_in, 16)
                    sp.dma_start(memv[:, :], mem_v).then_inc(inputs_in, 16)
                    with nc.allow_non_contiguous_dma(reason="a kilobyte of per-channel constants"):
                        sp.dma_start(bias[:, :], bg.rearrange("(a p) -> p a", p=P)).then_inc(inputs_in, 16)
                        for k in range(2):
                            sp.dma_start(hscale[k * DH:(k + 1) * DH, :], head_scale.rearrange(
                                "(a k) -> k a", k=2)[k:k + 1, :].to_broadcast([DH, PAIRS])).then_inc(inputs_in, 16)
                    for n in normed:
                        kind, c, m = tiles[n]
                        if kind == "q":
                            sp.wait_ge(turned_read, order[n] + 1)
                            for k in range(2):
                                sp.dma_start(q_dram[2 * c + k], q_out[:, c % 2, :, 64 * k:64 * k + 64]).then_inc(
                                    q_stored[c % 2], 16)
                    for p in range(PAIRS):
                        sp.wait_ge(g_ready, p + 1)
                        sp.dma_start(gate_dram[:, p, :], gates[:, p % 2, :]).then_inc(g_stored[p % 2], 16)
                    for k in range(2):
                        sp.wait_ge(q_stored[k], 16 * NT)
                        sp.wait_ge(g_stored[k], 16 * PAIRS // 2)

                @block.vector
                def _(dve):
                    v = nc.vector
                    steps = Counter(dve, dve_step)
                    v.memset(xT[:, 0:MEM], 0.0).then_inc(zero_ready, 1)
                    layer_norm(v, steps.link, range(NT), stats, mv, std, rstd, xn, var_ready,
                               std_ready).then_inc(xn_ready, 1)
                    for k, n in enumerate(normed):
                        kind, c, m = tiles[n]
                        dve.wait_ge(sq_ready, k + 1)
                        v.tensor_reduce(ss[0:m, k % 2, :], sq[0:m, k % 2, :].rearrange("p (h d) -> p h d", h=H),
                                        AX_X, ALU.add).then_inc(ss_ready, 1)
                        dve.wait_ge(nrm_ready, k + 1)
                        nk = nrm[0:m, k % 2, :]
                        rk = rnrm[0:m, k % 2, :]
                        steps.link(v.tensor_scalar(nk, nk, NORM_EPS, None, ALU.max))
                        steps.link(v.reciprocal(rk, nk))
                        if kind == "q":
                            steps.link(v.tensor_scalar(rk, rk, QK_SCALE, None, ALU.mult))
                        if k >= 2:
                            dve.wait_ge(turned_ready, k - 1)
                        v.tensor_tensor(rows_n[0:m, k % 2, :].rearrange("p (h d) -> p h d", h=H),
                                        proj[0:m, n % 2, :].rearrange("p (h d) -> p h d", h=H),
                                        rk.unsqueeze(2).to_broadcast([m, H, DH]), ALU.mult).then_inc(rows_ready, 1)
                    dve.wait_ge(inputs_in, 16 * 9)
                    for p in range(PAIRS):
                        dve.wait_ge(g_sig, p + 1)
                        v.tensor_scalar(gates[:, p % 2, :], gates[:, p % 2, :], hscale[:, p:p + 1], None,
                                        ALU.mult).then_inc(g_ready, 1)

                @block.scalar
                def _(act):
                    a = nc.scalar
                    act.wait_ge(var_ready, 1)
                    a.activation(std[:, :], std[:, :], ACT.Sqrt).then_inc(std_ready, 1)
                    for k in range(2):
                        act.wait_ge(xnT_ready, k + 1)
                        a.activation(xT[:, MEM + 4 * P * k:MEM + 4 * P * (k + 1)], turned[:, k, 0:BANK],
                                     ACT.Copy).then_inc(xT_ready, 1)

                    def copy_turned(k):
                        kind, c, m = tiles[normed[k]]
                        act.wait_ge(turned_ready, k + 1)
                        src = turned[:, k % 2, :].rearrange("p (a r) -> p a r", r=P)[:, :, 0:m]
                        if kind == "k":
                            dst = kT[:, :, c * P:c * P + m]
                        else:
                            if c >= 2:
                                act.wait_ge(q_stored[c % 2], 32 * (c // 2))
                            dst = q_out[:, c % 2, :, :]
                        a.activation(dst, src, ACT.Copy).then_inc(turned_read, 1)

                    for n, (kind, c, m) in enumerate(tiles):
                        act.wait_ge(proj_ready, n + 1)
                        if kind == "v":
                            a.activation(v_sb[0:m, c, :], proj[0:m, n % 2, :], ACT.Copy).then_inc(proj_read, 1)
                        elif kind == "g":
                            if c >= 2:
                                act.wait_ge(g_stored[c % 2], 16 * (c // 2))
                            act.wait_ge(inputs_in, 16 * 9)
                            a.activation(gates[:, c % 2, :], proj[:, n % 2, :], ACT.Sigmoid,
                                         bias=bias[:, c:c + 1]).then_inc(g_sig, 1)
                        else:
                            k = order[n]
                            a.activation(sq[0:m, k % 2, :], proj[0:m, n % 2, :], ACT.Square).then_inc(sq_ready, 1)
                            if k >= 1:
                                copy_turned(k - 1)
                            act.wait_ge(ss_ready, k + 1)
                            a.activation(nrm[0:m, k % 2, :], ss[0:m, k % 2, :], ACT.Sqrt).then_inc(nrm_ready, 1)
                            if k == len(normed) - 1:
                                copy_turned(k)

                @block.tensor
                def _(pe):
                    te = nc.tensor
                    pe.wait_ge(xn_ready, 1)
                    for t in range(NT):
                        ins = te.transpose(turned[:, t // 4, (t % 4) * P:(t % 4 + 1) * P], xn[:, t, :], ident[:, :])
                        if t % 4 == 3:
                            ins.then_inc(xnT_ready, 1)
                    pe.wait_ge(inputs_in, 16 * 9)
                    pe.wait_ge(xT_ready, 2)
                    pe.wait_ge(zero_ready, 1)

                    def slot_free(n):
                        kind, c, m = tiles[n]
                        if kind == "v":
                            pe.wait_ge(proj_read, n + 1)
                        elif kind == "g":
                            pe.wait_ge(g_sig, c + 1)
                        else:
                            pe.wait_ge(rows_ready, order[n] + 1)

                    def turn(k):
                        kind, c, m = tiles[normed[k]]
                        pe.wait_ge(rows_ready, k + 1)
                        if k >= 2:
                            pe.wait_ge(turned_read, k - 1)
                        for p in range(PAIRS):
                            ins = te.transpose(turned[:, k % 2, p * P:p * P + m], rows_n[0:m, k % 2, p * P:(p + 1) * P],
                                               ident[0:m, 0:m])
                        ins.then_inc(turned_ready, 1)

                    for n, (kind, c, m) in enumerate(tiles):
                        if n >= 2:
                            slot_free(n - 2)
                        for s in range(2):
                            o = proj[0:m, n % 2, s * BANK:(s + 1) * BANK]
                            if kind == "g":
                                ins = te.matmul(o, w[3][:, c * P:(c + 1) * P], xT[:, MEM + s * BANK:MEM + (s + 1) * BANK],
                                                start=True, stop=True)
                                continue
                            a0 = c * P + (MEM if kind == "q" else 0)
                            mem = kind != "q" and c == 0
                            wt = w["vkq".index(kind)][:, s * BANK:(s + 1) * BANK]
                            ins = te.matmul(o, xT[:, a0:a0 + m], wt, start=True, stop=not mem)
                            if mem:
                                rows = (memv if kind == "v" else memk)[:, s * BANK:(s + 1) * BANK]
                                ins = te.matmul(o, ident[0:MEM, 0:P], rows, start=False, stop=True)
                        ins.then_inc(proj_ready, 1)
                        if n in order and order[n] >= 1:
                            turn(order[n] - 1)
                        if n == normed[-1]:
                            turn(len(normed) - 1)

        def attention(b, kT, v_sb):
            with ExitStack() as f:
                q_diag = sb(f, "a_q_diag", [P, PAIRS, P])
                gate_u = sb(f, "a_gate_u", [P, PAIRS, 64])
                o_gated = sb(f, "a_o_gated", [P, PAIRS, 64])
                w_o = sb(f, "a_w_o", [P, PAIRS, D])
                stage = sb(f, "a_stage", [P, 2, J])
                SLOTS = 12
                regrouped = sb(f, "a_regrouped", [P, SLOTS, J])
                mixed = sb(f, "a_mixed", [P, 3, J])
                probs = sb(f, "a_probs", [P, 3, J])
                attnT = sb(f, "a_attnT", [P, KC, H, 64])
                top = sb(f, "a_top", [P, 2, TOPK])
                negmax = sb(f, "a_negmax", [P, 2])
                total = sb(f, "a_total", [P, 2])
                rtotal = sb(f, "a_rtotal", [P, 2])
                post = sb(f, "a_post", [P, 2, P])
                qk_ps = ps(f, "a_qk_ps", [P, 2, BANK])
                mix_ps = ps(f, "a_mix_ps", [P, 2, BANK])
                at_ps = ps(f, "a_at_ps", [P, 2, BANK])
                pv_ps = ps(f, "a_pv_ps", [P, PAIRS, 64])
                o_ps = ps(f, "a_o_ps", [P, BANK])

                wo_in = sem("a_wo_in")
                zeroed = sem("a_zeroed")
                q_in = sem("a_q_in")
                gate_in = sem("a_gate_in")
                dve_step = sem("a_dve_step")
                qk_ready = sem("a_qk_ready")
                qk_staged = sem("a_qk_staged")
                moved = [[sem(f"a_moved{h}{s}") for s in range(2)] for h in range(3)]
                mix_ready = sem("a_mix_ready")
                mix_copied = sem("a_mix_copied")
                top_ready = sem("a_top_ready")
                exp_ready = sem("a_exp_ready")
                probs_ready = sem("a_probs_ready")
                rtotal_ready = sem("a_rtotal_ready")
                post_ready = sem("a_post_ready")
                at_ready = sem("a_at_ready")
                at_copied = sem("a_at_copied")
                at_done = sem("a_at_done")
                pv_ready = sem("a_pv_ready")
                gated = sem("a_gated")
                o_ready = sem("a_o_ready")
                added = sem("a_added")

                width = [MEM + 64 * (u + 1) for u in range(UNITS)]
                npiece = [len(pieces(wd)) for wd in width]
                T = UNITS * G

                def qk_count(u, p):
                    return sum(npiece[:u]) * PAIRS + npiece[u] * (p + 1)

                def mix_count(t):
                    return sum(npiece[:t // G]) * G + npiece[t // G] * (t % G + 1)

                def banks(u):
                    full = [c for c in chunks(width[u]) if c[1] == P]
                    rest = [c for c in chunks(width[u]) if c[1] < P]
                    return [full[a:a + 4] for a in range(0, len(full), 4)] + [[c] for c in rest]

                nbank = [len(banks(u)) for u in range(UNITS)]

                def at_count(t):
                    return sum(nbank[:t // G]) * G + nbank[t // G] * (t % G + 1)

                def next_pairs(t):
                    u, g = divmod(t, G)
                    return (u + 1, range(2 * (g - 4), 2 * (g - 4) + 2)) if g >= 4 and u + 1 < UNITS else (u, ())

                block = f.enter_context(nc.Block())

                @block.sync
                def _(sp):
                    sp.dma_start(w_o[:, :, :], wo.rearrange("(a p) n -> p a n", p=P)).then_inc(wo_in, 16)
                    sp.wait_ge(zeroed, 1)

                    def load_gate(u):
                        if u >= 1:
                            sp.wait_ge(gated, u)
                        sp.dma_start(gate_u[:, :, :], gate_dram[:, :, 64 * u:64 * u + 64]).then_inc(gate_in, 16)

                    for u in range(UNITS):
                        if u >= 1:
                            sp.wait_ge(qk_ready, qk_count(u - 1, PAIRS - 1))
                        for k in range(2):
                            sp.dma_start(q_diag[64 * k:64 * k + 64, :, 64 * k:64 * k + 64],
                                         q_dram[u, 64 * k:64 * k + 64]).then_inc(q_in, 16)
                        if u >= 1:
                            load_gate(u - 1)
                        for p in range(PAIRS):
                            sp.wait_ge(qk_staged, qk_count(u, p))
                            for g in range(G):
                                t = G * u + g
                                if p == 0 and g % 4 == 0 and t // 4 >= 3:
                                    sp.wait_ge(mix_ready, mix_count(4 * (t // 4 - 3) + 3))
                                sp.dma_start(regrouped[16 * p:16 * p + 16, t % SLOTS, 0:width[u]],
                                             stage[g:P:G, p % 2, 0:width[u]]).then_inc(
                                                 moved[t // 4 % 3][p % 2], 16)
                    load_gate(UNITS - 1)

                @block.gpsimd
                def _(pool):
                    nc.gpsimd.memset(q_diag[:, :, :], 0.0).then_inc(zeroed, 1)
                    for t in range(T):
                        pool.wait_ge(rtotal_ready, t + 1)
                        if t >= 2:
                            pool.wait_ge(at_done, t - 1)
                        nc.gpsimd.tensor_scalar(post[:, t % 2, :], mix_post[:, :], rtotal[:, t % 2:t % 2 + 1], None,
                                                ALU.mult).then_inc(post_ready, 1)

                @block.vector
                def _(dve):
                    v = nc.vector
                    steps = Counter(dve, dve_step)

                    def top64(t):
                        wd = width[t // G]
                        dve.wait_ge(mix_copied, mix_count(t))
                        if t >= 3:
                            dve.wait_ge(at_done, t - 2)
                        src = mixed[:, t % 3, 0:wd]
                        scratch = probs[:, t % 3, 0:wd]
                        for r in range(TOPK // 8):
                            eight = top[:, t % 2, 8 * r:8 * r + 8]
                            steps.link(v.max(eight, src))
                            if r < TOPK // 8 - 1:
                                steps.link(v.match_replace(out=scratch, in_to_replace=eight, in_values=src,
                                                           imm_value=GONE))
                            src = scratch
                        v.tensor_scalar(negmax[:, t % 2:t % 2 + 1], top[:, t % 2, 0:1], -1.0, None,
                                        ALU.mult).then_inc(top_ready, 1)

                    def mask(t):
                        wd = width[t // G]
                        dve.wait_ge(exp_ready, t + 1)
                        v.scalar_tensor_tensor(out=probs[:, t % 3, 0:wd], in0=mixed[:, t % 3, 0:wd],
                                               scalar=top[:, t % 2, TOPK - 1:TOPK], in1=probs[:, t % 3, 0:wd],
                                               op0=ALU.is_ge, op1=ALU.mult,
                                               accum_out=total[:, t % 2:t % 2 + 1]).then_inc(probs_ready, 1)
                        dve.wait_ge(probs_ready, t + 1)
                        v.reciprocal(rtotal[:, t % 2:t % 2 + 1], total[:, t % 2:t % 2 + 1]).then_inc(rtotal_ready, 1)

                    def gate(u):
                        dve.wait_ge(pv_ready, u + 1)
                        dve.wait_ge(gate_in, 16 * (u + 1))
                        v.tensor_tensor(o_gated[:, :, :], pv_ps[:, :, :], gate_u[:, :, :], ALU.mult).then_inc(gated, 1)

                    def add(u):
                        dve.wait_ge(o_ready, u + 1)
                        o = 64 * (u % 2)
                        rows = x_sb[o:o + 64, u // 2, :]
                        v.tensor_tensor(rows, o_ps[o:o + 64, 0:D], rows, ALU.add).then_inc(added, 1)

                    for t in range(T + 5):
                        if t < T:
                            top64(t)
                        if 1 <= t <= T:
                            mask(t - 1)
                        if t >= G and t % G == 2:
                            gate(t // G - 1)
                        if t >= G and t % G == 4:
                            add(t // G - 1)

                @block.scalar
                def _(act):
                    a = nc.scalar
                    staged, copied, turned = [0], [0], [0]

                    def stage_pair(u, p):
                        if p >= 2:
                            for h in (2 * u, 2 * u + 1):
                                act.wait_ge(moved[h % 3][p % 2], 64 * (4 * (h // 3) + p // 2))
                        elif u >= 1:
                            for h in (2 * u - 2, 2 * u - 1):
                                act.wait_ge(moved[h % 3][p % 2], 64 * 4 * (h // 3 + 1))
                        for a0, n in pieces(width[u]):
                            act.wait_ge(qk_ready, staged[0] + 1)
                            a.activation(stage[:, p % 2, a0:a0 + n], qk_ps[:, staged[0] % 2, 0:n],
                                         ACT.Copy).then_inc(qk_staged, 1)
                            staged[0] += 1

                    def copy_mixed(t):
                        if t >= 3:
                            act.wait_ge(probs_ready, t - 2)
                        for a0, n in pieces(width[t // G]):
                            act.wait_ge(mix_ready, copied[0] + 1)
                            a.activation(mixed[:, t % 3, a0:a0 + n], mix_ps[:, copied[0] % 2, 0:n],
                                         ACT.Copy).then_inc(mix_copied, 1)
                            copied[0] += 1

                    def exponentials(t):
                        wd = width[t // G]
                        act.wait_ge(top_ready, t + 1)
                        a.activation(probs[:, t % 3, 0:wd], mixed[:, t % 3, 0:wd], ACT.Exp,
                                     bias=negmax[:, t % 2:t % 2 + 1]).then_inc(exp_ready, 1)

                    def copy_attnT(t):
                        u, g = divmod(t, G)
                        if g == 0 and u >= 1:
                            act.wait_ge(pv_ready, u)
                        for bank in banks(u):
                            act.wait_ge(at_ready, turned[0] + 1)
                            m, c0, k = bank[0][1], bank[0][0] // P, len(bank)
                            for j in range(k):
                                ins = a.activation(
                                    attnT[0:m, c0 + j, :, g:64:G],
                                    at_ps[0:m, turned[0] % 2, j * P:(j + 1) * P].rearrange("p (h i) -> p h i", h=H),
                                    ACT.Copy)
                            ins.then_inc(at_copied, 1)
                            turned[0] += 1

                    for p in range(PAIRS):
                        stage_pair(0, p)
                    for t in range(T + 2):
                        if t < T:
                            copy_mixed(t)
                        if 1 <= t <= T:
                            exponentials(t - 1)
                        if t >= 2:
                            copy_attnT(t - 2)
                        if t < T:
                            u, todo = next_pairs(t)
                            for p in todo:
                                stage_pair(u, p)

                @block.tensor
                def _(pe):
                    te = nc.tensor
                    made, mixes, turned = [0], [0], [0]

                    def scores(u, p):
                        if p == 0:
                            pe.wait_ge(q_in, 32 * (u + 1))
                        for a0, n in pieces(width[u]):
                            if made[0] >= 2:
                                pe.wait_ge(qk_staged, made[0] - 1)
                            te.matmul(qk_ps[:, made[0] % 2, 0:n], q_diag[:, p, :], kT[:, p, a0:a0 + n],
                                      start=True, stop=True).then_inc(qk_ready, 1)
                            made[0] += 1

                    def mix(t):
                        u, g = divmod(t, G)
                        if g % 4 == 0:
                            h = t // 4
                            for s in range(2):
                                pe.wait_ge(moved[h % 3][s], 256 * (h // 3 + 1))
                        diag = width[u] - 64
                        for a0, n in pieces(width[u]):
                            if mixes[0] >= 2:
                                pe.wait_ge(mix_copied, mixes[0] - 1)
                            lo = max(diag, a0)
                            masked = lo < a0 + n
                            o = mix_ps[:, mixes[0] % 2, :]
                            ins = te.matmul(o[:, 0:n], mix_pre[:, :], regrouped[:, t % SLOTS, a0:a0 + n],
                                            start=True, stop=not masked)
                            if masked:
                                ins = te.matmul(o[:, lo - a0:n], row_sel[:, :], row_mask[:, g, lo - diag:a0 + n - diag],
                                                start=False, stop=True)
                            ins.then_inc(mix_ready, 1)
                            mixes[0] += 1

                    def turn(t):
                        pe.wait_ge(probs_ready, t + 1)
                        pe.wait_ge(post_ready, t + 1)
                        for bank in banks(t // G):
                            if turned[0] >= 2:
                                pe.wait_ge(at_copied, turned[0] - 1)
                            for j, (a0, m) in enumerate(bank):
                                ins = te.matmul(at_ps[0:m, turned[0] % 2, j * P:(j + 1) * P],
                                                probs[:, t % 3, a0:a0 + m], post[:, t % 2, :], start=True, stop=True)
                            ins.then_inc(at_ready, 1)
                            turned[0] += 1
                        pe.wait_ge(at_ready, turned[0])
                        pe.sem_inc(at_done, 1)

                    def values(u):
                        pe.wait_ge(at_copied, at_count(G * u + G - 1))
                        if u >= 1:
                            pe.wait_ge(gated, u)
                        cs = chunks(width[u])
                        for p in range(PAIRS):
                            for k in range(2):
                                h = 2 * p + k
                                for c, (a0, m) in enumerate(cs):
                                    ins = te.matmul(pv_ps[64 * k:64 * k + 64, p, :], v_sb[0:m, c, h * DH:(h + 1) * DH],
                                                    attnT[0:m, c, h, :], start=(c == 0), stop=(c == len(cs) - 1))
                        ins.then_inc(pv_ready, 1)

                    def project_out(u):
                        pe.wait_ge(gated, u + 1)
                        if u >= 1:
                            pe.wait_ge(added, u)
                        o = 64 * (u % 2)
                        for p in range(PAIRS):
                            ins = te.matmul(o_ps[o:o + 64, 0:D], o_gated[:, p, :], w_o[:, p, :],
                                            start=(p == 0), stop=(p == PAIRS - 1))
                        ins.then_inc(o_ready, 1)

                    pe.wait_ge(wo_in, 16)
                    for p in range(PAIRS):
                        scores(0, p)
                    for t in range(T + 5):
                        if t < T:
                            mix(t)
                        if 2 <= t < T + 2:
                            turn(t - 2)
                        if t < T:
                            u, todo = next_pairs(t)
                            for p in todo:
                                scores(u, p)
                        if t >= G and t % G == 1:
                            values(t // G - 1)
                        if t >= G and t % G == 3:
                            project_out(t // G - 1)

        with nc.Fori(0, B) as b:
            ffn(b, 0)
            with ExitStack() as kv:
                kT = sb(kv, "kT", [P, PAIRS, J])
                v_sb = sb(kv, "v_sb", [P, KC, HD])
                project(b, kT, v_sb)
                attention(b, kT, v_sb)
            ffn(b, 1)
            nc.clear_and_free_semaphores(all_sems[first_loop_sem:])
            nc.all_engine_barrier()


def setup_weights(nc, ctx, sb, ps, sem, ident, mix_pre, mix_post, row_sel, row_mask, wpreT, wpostT,
                  w_gate, w_up, w_down, w_gu_dram, w_dn_dram, I, ICH, BLK_X, BLK_H, G, H):
    NCH = len(ICH)
    with ExitStack() as f:
        nat = sb(f, "s_nat", [P, 3 * NCH, P])
        amax = sb(f, "s_amax", [P, 3 * NCH * 8])
        scale = sb(f, "s_scale", [P, 3 * NCH * 8])
        rscale = sb(f, "s_rscale", [P, 3 * NCH * 8])
        xs = sb(f, "s_xs", [P, 3 * NCH * P])
        mag = sb(f, "s_mag", [P, 3 * NCH * P])
        sign = sb(f, "s_sign", [P, 3 * NCH * P])
        level = sb(f, "s_level", [P, 3 * NCH * P])
        tmp = sb(f, "s_tmp", [P, 3 * NCH * P])
        wqz = sb(f, "s_wqz", [P, 3 * NCH * P])
        wT = sb(f, "s_wT", [P, 3, NCH * P])
        tp = ps(f, "s_tp", [P, 3, BANK])
        zeroed = sem("s_zeroed")
        pool_step = sem("s_pool_step")
        consts = sem("s_consts")
        loaded = sem("s_loaded")
        mixes_in = sem("s_mixes_in")
        dve_step = sem("s_dve_step")
        scaled = sem("s_scaled")
        mag_ready = sem("s_mag_ready")
        quantised = sem("s_quantised")
        turned = sem("s_turned")
        copied = sem("s_copied")
        stored = sem("s_stored")
        block = f.enter_context(nc.Block())

        @block.sync
        def _(sp):
            sp.wait_ge(zeroed, 3)
            for k, src in enumerate((w_gate, w_up)):
                for c, (a0, m) in enumerate(ICH):
                    sp.dma_start(nat[0:m, NCH * k + c, :], src[a0:a0 + m, :]).then_inc(loaded, 16)
            sp.dma_start(nat[:, 2 * NCH:3 * NCH, :].rearrange("p c k -> p (c k)")[:, 0:I], w_down).then_inc(loaded, 16)
            with nc.allow_non_contiguous_dma(reason="two 16 x 16 matrices, spread over the diagonals of 8 x 8 blocks"):
                for dst, src in ((mix_pre, wpreT), (mix_post, wpostT)):
                    for i in range(G):
                        sp.dma_start(dst[i:P:G, i:P:G], src).then_inc(mixes_in, 16)
            sp.wait_ge(copied, 3)
            sp.dma_start(w_gu_dram[:, 0:I], wT[:, 0, 0:I]).then_inc(stored, 16)
            sp.dma_start(w_gu_dram[:, I:2 * I], wT[:, 1, 0:I]).then_inc(stored, 16)
            sp.dma_start(w_dn_dram, wT[:, 2, :].rearrange("p (c k) -> p c k", k=P)).then_inc(stored, 16)
            sp.wait_ge(stored, 48)
            sp.wait_ge(mixes_in, 16 * 2 * G)

        @block.gpsimd
        def _(pool):
            g = nc.gpsimd
            g.memset(ident[:, :], 0.0).then_inc(pool_step, 1)
            g.memset(row_sel[:, :], 0.0).then_inc(pool_step, 1)
            g.memset(row_mask[:, :, :], 0.0).then_inc(pool_step, 1)
            g.memset(wT[:, :, :], 0.0).then_inc(zeroed, 1)
            pool.wait_ge(pool_step, 3)
            g.affine_select(out=ident[:, :], in_=ident[:, :], compare_op=ALU.not_equal, fill=1.0, base=0,
                            pattern=[[-1, P]], channel_multiplier=1).then_inc(consts, 1)
            rs = row_sel[:, :].rearrange("k (h i) -> k h i", h=H)
            g.affine_select(out=rs, in_=rs, compare_op=ALU.not_equal, fill=1.0, base=0,
                            pattern=[[0, H], [-1, G]], channel_multiplier=1).then_inc(consts, 1)
            g.affine_select(out=row_mask[:, :, :], in_=row_mask[:, :, :], compare_op=ALU.is_ge, fill=NEG, base=0,
                            pattern=[[1, G], [-1, 64]], channel_multiplier=8).then_inc(consts, 1)

        @block.vector
        def _(dve):
            v = nc.vector
            steps = Counter(dve, dve_step)
            v.memset(nat[:, :, :], 0.0).then_inc(zeroed, 1)
            steps.link(v.memset(mix_pre[:, :], 0.0))
            v.memset(mix_post[:, :], 0.0).then_inc(zeroed, 1)
            dve.wait_ge(loaded, 16 * (2 * NCH + 1))
            n3 = nat[:, :, :].rearrange("p c (n e) -> p (c n) e", e=QBLOCK)
            quantise_scale(steps.link, v, n3, amax[:, :], scale[:, :], rscale[:, :])
            nb = 3 * NCH * 8
            v.tensor_tensor(xs[:, :].rearrange("p (n e) -> p n e", e=QBLOCK), n3,
                            rscale[:, :].unsqueeze(2).to_broadcast([P, nb, QBLOCK]), ALU.mult).then_inc(scaled, 1)
            dve.wait_ge(mag_ready, 1)
            quantise_levels(steps.link, v, mag[:, :], level[:, :], tmp[:, :])
            dve.wait_ge(mag_ready, 2)
            s3 = sign[:, :].rearrange("p (n e) -> p n e", e=QBLOCK)
            steps.link(v.tensor_tensor(s3, s3, scale[:, :].unsqueeze(2).to_broadcast([P, nb, QBLOCK]), ALU.mult))
            v.tensor_tensor(wqz[:, :], level[:, :], sign[:, :], ALU.mult).then_inc(quantised, 1)

        @block.scalar
        def _(act):
            a = nc.scalar
            act.wait_ge(scaled, 1)
            a.activation(mag[:, :], xs[:, :], ACT.Abs).then_inc(mag_ready, 1)
            a.activation(sign[:, :], xs[:, :], ACT.Sign).then_inc(mag_ready, 1)
            act.wait_ge(zeroed, 3)
            for k in range(2):
                act.wait_ge(turned, k + 1)
                a.activation(wT[:, k, 0:I], tp[:, k, 0:I], ACT.Copy).then_inc(copied, 1)
            act.wait_ge(turned, 3)
            a.activation(wT[:, 2, 0:(NCH - 1) * P], tp[:, 2, 0:(NCH - 1) * P], ACT.Copy)
            r = ICH[-1][1]
            a.activation(wT[0:r, 2, (NCH - 1) * P:], tp[0:r, 2, (NCH - 1) * P:NCH * P], ACT.Copy).then_inc(copied, 1)

        @block.tensor
        def _(pe):
            te = nc.tensor
            pe.wait_ge(quantised, 1)
            pe.wait_ge(consts, 3)
            for k in range(2):
                for c, (a0, m) in enumerate(ICH):
                    o = (NCH * k + c) * P
                    ins = te.transpose(tp[:, k, a0:a0 + m], wqz[0:m, o:o + P], ident[0:m, 0:m])
                ins.then_inc(turned, 1)
            for c, (a0, m) in enumerate(ICH):
                o = 2 * NCH * P + a0
                ins = te.transpose(tp[0:m, 2, c * P:(c + 1) * P], wqz[:, o:o + m], ident[:, :])
            ins.then_inc(turned, 1)


def kernel(**inputs):
    import numpy as _np
    import concourse.bacc as _bacc
    from concourse import mybir as _mybir
    from concourse.bass_utils import run_bass_kernel_spmd as _run

    a = {k.replace("L0_attn_", "").replace("L0_ffn_", ""): _np.ascontiguousarray(v) for k, v in inputs.items()}
    heads, mem, dh = a["mem_k"].shape
    laid = {
        "x": a["x"], "wq": a["Wq"], "wk": a["Wk"], "wv": a["Wv"],
        "wpreT": _np.ascontiguousarray(a["W_pre_th"].T), "wpostT": _np.ascontiguousarray(a["W_post_th"].T),
        "mem_k": _np.ascontiguousarray(a["mem_k"].transpose(1, 0, 2).reshape(mem, heads * dh)),
        "mem_v": _np.ascontiguousarray(a["mem_v"].transpose(1, 0, 2).reshape(mem, heads * dh)),
        "head_scale": a["head_scale_params"].reshape(heads), "wg": a["Wg"], "bg": a["bg"], "wo": a["Wo"],
        "w_gate": a["w_gate"], "w_up": a["w_up"], "w_down": a["w_down"],
    }
    nc = _bacc.Bacc("TRN2", target_bir_lowering=False, num_devices=1)
    arrays, args = {}, []
    for name, arr in laid.items():
        arrays[f"in_{name}_dram"] = arr
        args.append(nc.dram_tensor(f"in_{name}_dram", arr.shape, _mybir.dt.from_np(arr.dtype), kind="ExternalInput").ap())
    args.append(nc.dram_tensor("out_0_dram", a["x"].shape, _mybir.dt.float32, kind="ExternalOutput").ap())
    macaron_kernel(nc, *args)
    r = _run(nc, [arrays], core_ids=[0])
    return r.results[0]["out_0_dram"]
```
